# Optimizing a Trainium2 kernel written in Bass

```python
import numpy as np
import jax
import jax.numpy as jnp

def _softmax(x, axis=-1):
    return jax.nn.softmax(x, axis=axis)

def _gelu(x):
    return jax.nn.gelu(x, approximate=True)

def _silu(x):
    return jax.nn.silu(x)

def _sigmoid(x):
    return jax.nn.sigmoid(x)

def _layernorm(x, axis=-1, eps=1e-05):
    m = jnp.mean(x, axis=axis, keepdims=True)
    v = jnp.var(x, axis=axis, keepdims=True)
    return (x - m) / jnp.sqrt(v + eps)

def _scatter_add(tgt, idx, src, axis=0):
    return tgt.at[idx].add(src)

def _segment_sum(src, seg, n):
    return jax.ops.segment_sum(src, seg, n)
kernel_name = 'mk_cond_resid_d2_seqx_r4_56b5e0'

def setup_inputs(seed: int=0):
    np.random.seed(seed)
    _w = jnp.asarray

    def _rec_inputs():
        import jax
        import jax.numpy as jnp
        _rk = jax.random.key(seed)
        x = -0.000125 + 0.9999 * jax.random.normal(jax.random.fold_in(_rk, 1), (128, 64, 512), jnp.float32)
        _lenS = 64 - jax.random.randint(jax.random.fold_in(_rk, 7), (128,), 0, max(1, 64 // 4) + 1, jnp.int32)
        _lenS2 = 64 - jax.random.randint(jax.random.fold_in(_rk, 8), (128,), 0, max(1, 64 // 4) + 1, jnp.int32)
        cond_2048 = 0.000782532 + 0.100527 * jax.random.normal(jax.random.fold_in(_rk, 11), (128, 512), jnp.float32)
        return (x, cond_2048)
    x, cond_2048 = _rec_inputs()

    def _L0_cond_setup():
        import jax, jax.numpy as jnp
        import numpy as np
        key = jax.random.key(seed)
        k1, k2, k3 = jax.random.split(key, 3)
        B, L, D, K = (4, 1024, 512, 4)
        x = jax.random.normal(k1, (B, L, D), dtype=jnp.float32)
        w = jax.random.normal(k2, (K, 1, D), dtype=jnp.float32) * 0.1
        b = jax.random.normal(k3, (D,), dtype=jnp.float32) * 0.1
        return {'x': x, 'w': w, 'b': b}
    _L0_cond_all = _L0_cond_setup()
    _L0_cond_in = {k: v for k, v in _L0_cond_all.items() if k in ('b',)}
    del _L0_cond_all

    def _L1_cond_setup():
        import jax, jax.numpy as jnp
        import numpy as np
        B, T, D = (16, 128, 512)
        key = jax.random.key(seed)
        k0, k1, k2, k3 = jax.random.split(key, 4)
        scale = 1.0 / np.sqrt(D)
        return {'initial_state': jax.random.normal(k0, (B, D), jnp.float32), 'inputs': jax.random.normal(k1, (B, T, D), jnp.float32), 'W_ih': jax.random.normal(k2, (D, 3 * D), jnp.float32) * scale, 'W_hh': jax.random.normal(k3, (D, 3 * D), jnp.float32) * scale, 'b_ih': jnp.zeros((3 * D,), jnp.float32), 'b_hh': jnp.zeros((3 * D,), jnp.float32)}
    _L1_cond_all = _L1_cond_setup()
    _L1_cond_in = {k: v for k, v in _L1_cond_all.items() if k in ('W_ih', 'W_hh', 'b_ih', 'b_hh')}
    del _L1_cond_all
    return {'x': x, 'cond_2048': cond_2048, 'L0_cond_b': _L0_cond_in['b'], 'L1_cond_W_ih': _L1_cond_in['W_ih'], 'L1_cond_W_hh': _L1_cond_in['W_hh'], 'L1_cond_b_ih': _L1_cond_in['b_ih'], 'L1_cond_b_hh': _L1_cond_in['b_hh']}

def reference(x, cond_2048, L0_cond_b, L1_cond_W_ih, L1_cond_W_hh, L1_cond_b_ih, L1_cond_b_hh):
    import jax
    import jax.numpy as jnp

    def _L0_cond_ref(x, w, b):
        import jax, jax.numpy as jnp
        import numpy as np
        'Depthwise causal conv1d, channel-last.\n            x: (B, L, D); w: (K, 1, D); b: (D,). Returns (B, L, D).\n            Matches torch: Conv1d(D, D, K, groups=D, padding=K-1)(x.T)[..., :L].T\n            which is exactly a causal conv (left pad K-1, trim to L).\n            '
        K = w.shape[0]
        D = x.shape[-1]
        y = jax.lax.conv_general_dilated(x, w, window_strides=(1,), padding=[(K - 1, 0)], feature_group_count=D, dimension_numbers=('NWC', 'WIO', 'NWC'))
        return y + b

    def _L1_cond_ref(initial_state, inputs, W_ih, W_hh, b_ih, b_hh):
        import jax, jax.numpy as jnp
        import numpy as np
        B, T, D = (16, 128, 512)
        "ScanOverTime(GRU cell): sequential per-timestep module call with\n            dict-state passing; merge_dict_trees stacks the per-step\n            'state_predicted' tensors along axis=1 -> [B, T, D]."

        def cell(h, x):
            gi = x @ W_ih + b_ih
            gh = h @ W_hh + b_hh
            i_r, i_z, i_n = jnp.split(gi, 3, axis=-1)
            h_r, h_z, h_n = jnp.split(gh, 3, axis=-1)
            r = jax.nn.sigmoid(i_r + h_r)
            z = jax.nn.sigmoid(i_z + h_z)
            n = jnp.tanh(i_n + r * h_n)
            h_new = (1.0 - z) * n + z * h
            return (h_new, h_new)
        xs = jnp.swapaxes(inputs, 0, 1)
        _, hs = jax.lax.scan(cell, initial_state, xs)
        return jnp.swapaxes(hs, 0, 1)
    x = x + _L0_cond_ref(x, cond_2048[:, None, :], L0_cond_b)
    x = x + _L1_cond_ref(cond_2048, x, L1_cond_W_ih, L1_cond_W_hh, L1_cond_b_ih, L1_cond_b_hh)
    return x

_drawn_inputs = setup_inputs


def setup_inputs(seed=0):
    import zlib

    import numpy as np

    out = dict(_drawn_inputs(seed))
    spreads = {'L1_cond_b_ih': (0.0, 0.1), 'L1_cond_b_hh': (0.0, 0.272)}
    factors = {}
    for name, (base, spread) in spreads.items():
        noise = np.random.default_rng([zlib.crc32(name.encode()), seed]).standard_normal(out[name].shape)
        drawn = base * np.exp(spread * noise) if base else spread * noise
        out[name] = jnp.asarray(drawn.astype(out[name].dtype))
    for name, factor in factors.items():
        out[name] = (out[name] * factor).astype(out[name].dtype)
    return out
```

```python
from contextlib import ExitStack

import concourse.bass as bass
from concourse import mybir

P = 128
F32 = mybir.dt.float32
F32R = mybir.dt.float32r
ALU = mybir.AluOpType
ACT = mybir.ActivationFunctionType

KW = 4
RING = 4
SLICE = 32
PIECE = 8
BANK = 512


def conv_residual_gru(
    nc: bass.Bass,
    x: bass.AP,
    taps: bass.AP,
    conv_b: bass.AP,
    w_ih: bass.AP,
    w_hh: bass.AP,
    b_ih: bass.AP,
    b_hh: bass.AP,
    out: bass.AP,
):
    B, T, D = x.shape
    K = taps.shape[0]
    NG = w_ih.shape[1]
    assert B == P and 2 * T == P and NG == 3 * D and D == BANK and K >= T and taps.shape[1] == D
    KB = D // P
    CH = D // (2 * P)
    GROUPS = P // SLICE
    PIECES = SLICE // PIECE
    NPIECE = CH * GROUPS * PIECES
    BPAIRS = BANK // P
    NBANK = CH * P // BPAIRS
    PBANKS = PIECE // BPAIRS
    STRIPS = P // SLICE

    def x_strip(k, q):
        c, g = k // 2, k % 2 * 2 + q // 2
        return c * 2 * P + q % 2 * P + g * SLICE

    R, Z, N = 0, D, 2 * D

    tap_rows = nc.dram_tensor("tap_rows", [2 * T, D], F32, kind="Internal").ap()
    xres = nc.dram_tensor("xres", [CH * GROUPS, B, T, 2 * SLICE], F32, kind="Internal").ap()

    BASE = 2048
    top = [BASE]

    def place(name, cols, dtype=F32, parts=P):
        t = nc.alloc_sbuf_tensor_at(name, [parts, cols], dtype, offset=top[0])
        top[0] += cols * KW
        return t

    x_at = top[0]
    x_sb = [place(f"x_sb{c}", B * P) for c in range(CH)]
    toep_at = top[0]
    toep = [place(f"toep{c}", T * P) for c in range(CH)]
    diag = [place(f"diag{n}", PIECE * P) for n in range(2)]
    stage_at = top[0]
    stage = place("stage", T * 2 * SLICE)
    conv_bias = place("conv_bias", D)
    ident = place("ident", P)
    assert top[0] <= nc.SBUF_PARTITION_SIZE_BYTES - 64

    top[0] = stage_at
    lag0 = place("lag0", D, parts=1)
    zeros = place("zeros", D, parts=T)

    hi, lo, raw = [], [], []
    for c, name in enumerate(("ih", "hh")):
        top[0] = x_at + c * B * P * KW
        hi.append(place(f"w_{name}_hi", KB * NG, F32R))
        lo.append(place(f"w_{name}_lo", KB * NG, F32R))
        raw.append([place(f"w_{name}_raw{n}", NG) for n in range(2)])
        assert top[0] <= x_at + (c + 1) * B * P * KW

    top[0] = toep_at
    h = place("h", D)
    xt = [place(f"xt{n}", D) for n in range(RING)]
    out_t = [place(f"out_t{n}", D) for n in range(RING)]
    hT_hi, hT_lo, xT_hi, xT_lo = (place(n, D, F32R) for n in ("hT_hi", "hT_lo", "xT_hi", "xT_lo"))
    pre_r, pre_z, r, z, n_gate = (place(n, D) for n in ("pre_r", "pre_z", "r", "z", "n_gate"))
    new_h, new_x, reset_h, pre_n = (place(n, D) for n in ("new_h", "new_x", "reset_h", "pre_n"))
    h_less_n, z_part = place("h_less_n", D), place("z_part", D)
    bias_ih, bias_hh, bias_rz = place("bias_ih", NG), place("bias_hh", NG), place("bias_rz", 2 * D)
    assert top[0] <= toep_at + CH * T * P * KW

    ctx = ExitStack()
    with ctx:
        bank = [ctx.enter_context(nc.psum_tensor(f"bank{n}", [P, BANK], F32)) for n in range(8)]
        ps_r, ps_z, ps_in, ps_hn, ps_xT, ps_hT = bank[:6]

        def sem(name):
            return ctx.enter_context(nc.semaphore(name))

        lag0_loaded = sem("lag0_loaded")
        lag0_plus_one = sem("lag0_plus_one")
        zeros_set = sem("zeros_set")
        tap_rows_stored = sem("tap_rows_stored")
        x_loaded = [sem(f"x_loaded{c}") for c in range(CH)]
        toep_loaded = [sem(f"toep_loaded{c}") for c in range(CH)]
        bias_loaded = sem("bias_loaded")
        diag_zeroed = sem("diag_zeroed")
        ident_set = sem("ident_set")
        diag_ready = sem("diag_ready")
        conv_done = sem("conv_done")
        stage_ready = sem("stage_ready")
        xres_stored = sem("xres_stored")
        raw_loaded = [[sem(f"raw_loaded{c}{n}") for n in range(2)] for c in range(2)]
        w_hi_ready = sem("w_hi_ready")
        w_lo_ready = sem("w_lo_ready")
        h0_loaded = sem("h0_loaded")
        gate_bias_loaded = sem("gate_bias_loaded")
        bias_rz_ready = sem("bias_rz_ready")
        xt_loaded = [sem(f"xt_loaded{n}") for n in range(RING)]
        xT_done = sem("xT_done")
        xT_hi_ready = sem("xT_hi_ready")
        xT_lo_ready = sem("xT_lo_ready")
        hT_done = sem("hT_done")
        hT_hi_ready = sem("hT_hi_ready")
        hT_lo_ready = sem("hT_lo_ready")
        gi_done = sem("gi_done")
        gh_r_done = sem("gh_r_done")
        gh_n_done = sem("gh_n_done")
        gh_z_done = sem("gh_z_done")
        new_x_ready = sem("new_x_ready")
        pre_r_ready = sem("pre_r_ready")
        r_ready = sem("r_ready")
        new_h_ready = sem("new_h_ready")
        reset_h_ready = sem("reset_h_ready")
        pre_n_ready = sem("pre_n_ready")
        n_ready = sem("n_ready")
        h_less_n_ready = sem("h_less_n_ready")
        pre_z_ready = sem("pre_z_ready")
        z_ready = sem("z_ready")
        z_part_ready = sem("z_part_ready")
        h_ready = sem("h_ready")
        out_ready = sem("out_ready")
        out_stored = [sem(f"out_stored{n}") for n in range(RING)]

        ROUNDS = T // RING
        assert T % RING == 0 and ROUNDS >= 3

        def rounds(eng, first, body):
            if first:
                for u in range(RING):
                    body(0, u)
            with eng.Fori(1 if first else 0, ROUNDS - 1) as i:
                for u in range(RING):
                    body(i, u)
            for u in range(RING):
                body(ROUNDS - 1, u)

        def last(i, u):
            return not isinstance(i, bass.RuntimeValue) and i == ROUNDS - 1 and u == RING - 1

        block = ctx.enter_context(nc.Block())

        @block.sync
        def _(sp):
            for c in range(CH):
                for half in range(2):
                    ch = (2 * c + half) * P
                    sp.dma_start(
                        x_sb[c][half * T:(half + 1) * T, :].rearrange("s (b i) -> s b i", b=B),
                        x[:, :, ch:ch + P].rearrange("b s i -> s b i"),
                    ).then_inc(x_loaded[c], 16)
            for g in range(CH * GROUPS):
                sp.wait_ge(stage_ready, (g + 1) * NBANK // (CH * GROUPS))
                sp.dma_start(xres[g].rearrange("b u e -> b (u e)"), stage[:, :]).then_inc(xres_stored, 16)
            sp.wait_ge(xres_stored, 16 * CH * GROUPS)
            for t in range(RING):
                sp.dma_start(
                    xt[t][:, :].rearrange("b (g e) -> b g e", g=CH * GROUPS),
                    xres[:, :, T - 1 - t, :].rearrange("g b e -> b g e"),
                ).then_inc(xt_loaded[t], 16)

            def step(i, u):
                sp.wait_ge(out_ready, i * RING + u + 1)
                t = i * RING + u
                sp.dma_start(out[:, bass.ds(t, 1), :].rearrange("b o d -> b (o d)"),
                             out_t[u][:, :]).then_inc(out_stored[u], 16)
                if isinstance(i, bass.RuntimeValue) or i < ROUNDS - 1:
                    back = T - 1 - RING - u - i * RING
                    sp.dma_start(
                        xt[u][:, :].rearrange("b (g o e) -> b g o e", g=CH * GROUPS, o=1),
                        xres[:, :, bass.ds(back, 1), :].rearrange("g b o e -> b g o e"),
                    ).then_inc(xt_loaded[u], 16)

            rounds(sp, False, step)
            for u in range(RING):
                sp.wait_ge(out_stored[u], 16 * ROUNDS)

        @block.gpsimd
        def _(pool):
            nc.gpsimd.memset(zeros[:, :], 0.0).then_inc(zeros_set, 1)
            for n in range(2):
                nc.gpsimd.memset(diag[n][:, :], 0.0).then_inc(diag_zeroed, 1)
            nc.gpsimd.memset(ident[:, :], 0.0).then_inc(ident_set, 1)
            pool.wait_ge(ident_set, 1)
            nc.gpsimd.affine_select(out=ident[:, :], in_=ident[:, :], compare_op=ALU.not_equal, fill=1.0,
                                    base=0, pattern=[[-1, P]], channel_multiplier=1).then_inc(ident_set, 1)

        @block.scalar
        def _(act):
            act.dma_start(lag0[:, :], taps[K - 1:K, :]).then_inc(lag0_loaded, 16)
            act.dma_start(conv_bias[:, :], conv_b.partition_broadcast(P)).then_inc(bias_loaded, 16)
            act.dma_start(tap_rows[0:T - 1, :], taps[K - T:K - 1, :]).then_inc(tap_rows_stored, 16)
            act.wait_ge(zeros_set, 1)
            act.dma_start(tap_rows[T:2 * T, :], zeros[:, :]).then_inc(tap_rows_stored, 16)
            act.wait_ge(lag0_plus_one, 1)
            act.dma_start(tap_rows[T - 1:T, :], lag0[:, :]).then_inc(tap_rows_stored, 16)
            act.wait_ge(tap_rows_stored, 48)
            for c in range(CH):
                for half in range(2):
                    ch = (2 * c + half) * P
                    src = tap_rows[0:T, ch:ch + P]
                    src = bass.AP(src.tensor, src.offset, [[D, T], [D, T], [1, P]])
                    act.dma_start(toep[c][half * T:(half + 1) * T, :].rearrange("s (u i) -> s u i", u=T),
                                  src).then_inc(toep_loaded[c], 16)

            def load_weights(c, w, k):
                for q in range(STRIPS):
                    row = x_strip(k, q) if c == 0 else k * P + q * SLICE
                    act.dma_start(raw[c][k % 2][q * SLICE:(q + 1) * SLICE, :],
                                  w[row:row + SLICE, :]).then_inc(raw_loaded[c][k % 2], 16)

            def split_hi(c, w, k):
                act.wait_ge(raw_loaded[c][k % 2], 16 * STRIPS * (k // 2 + 1))
                for q in range(NG // BANK):
                    m = nc.scalar.activation(hi[c][:, k * NG + q * BANK:k * NG + (q + 1) * BANK],
                                             raw[c][k % 2][:, q * BANK:(q + 1) * BANK], ACT.Copy)
                m.then_inc(w_hi_ready, 1)
                if k + 2 < KB:
                    act.wait_ge(w_lo_ready, c * KB + k + 1)
                    load_weights(c, w, k + 2)

            act.wait_ge(diag_zeroed, 2)
            for p in range(NPIECE):
                c, i0 = p // (NPIECE // CH), p % (NPIECE // CH) * PIECE
                if p % (NPIECE // CH) == 0:
                    act.wait_ge(toep_loaded[c], 32)
                if p >= 2:
                    act.wait_ge(conv_done, (p - 1) * PBANKS)
                for half in range(2):
                    rows = slice(half * T, (half + 1) * T)
                    m = nc.scalar.activation(
                        diag[p % 2][rows, :].rearrange("s (i h u) -> s i h u", i=PIECE, h=2)[:, :, half, :],
                        toep[c][rows, :].rearrange("s (u i) -> s i u", u=T)[:, i0:i0 + PIECE, :], ACT.Copy)
                m.then_inc(diag_ready, 1)
                if p == NPIECE // 2 + 2:
                    for k in range(2):
                        load_weights(0, w_ih, k)
                if p >= NPIECE - KB:
                    split_hi(0, w_ih, p - (NPIECE - KB))
            act.wait_ge(conv_done, NBANK)
            for k in range(2):
                load_weights(1, w_hh, k)
            act.dma_start(h[:, :], taps).then_inc(h0_loaded, 16)
            act.dma_start(bias_ih[:, :], b_ih.partition_broadcast(P)).then_inc(gate_bias_loaded, 16)
            act.dma_start(bias_hh[:, :], b_hh.partition_broadcast(P)).then_inc(gate_bias_loaded, 16)
            for k in range(KB):
                split_hi(1, w_hh, k)

            act.wait_ge(hT_done, 1)
            nc.scalar.activation(hT_hi[:, :], ps_hT[:, :], ACT.Copy).then_inc(hT_hi_ready, 1)
            act.wait_ge(xT_done, 1)
            nc.scalar.activation(xT_hi[:, :], ps_xT[:, :], ACT.Copy).then_inc(xT_hi_ready, 1)

            def step(i, u):
                t = i * RING + u
                act.wait_ge(pre_r_ready, t + 1)
                nc.scalar.activation(r[:, :], pre_r[:, :], ACT.Sigmoid).then_inc(r_ready, 1)
                if not last(i, u):
                    act.wait_ge(xT_done, t + 2)
                    nc.scalar.activation(xT_hi[:, :], ps_xT[:, :], ACT.Copy).then_inc(xT_hi_ready, 1)
                act.wait_ge(pre_n_ready, t + 1)
                nc.scalar.activation(n_gate[:, :], pre_n[:, :], ACT.Tanh).then_inc(n_ready, 1)
                act.wait_ge(pre_z_ready, t + 1)
                nc.scalar.activation(z[:, :], pre_z[:, :], ACT.Sigmoid).then_inc(z_ready, 1)
                if not last(i, u):
                    act.wait_ge(hT_done, t + 2)
                    nc.scalar.activation(hT_hi[:, :], ps_hT[:, :], ACT.Copy).then_inc(hT_hi_ready, 1)

            rounds(act, False, step)

        @block.vector
        def _(dve):
            dve.wait_ge(lag0_loaded, 16)
            nc.vector.tensor_scalar_add(lag0[:, :], lag0[:, :], 1.0).then_inc(lag0_plus_one, 1)
            dve.wait_ge(bias_loaded, 16)

            def split_lo(c, k):
                dve.wait_ge(w_hi_ready, c * KB + k + 1)
                for q in range(NG // BANK):
                    cols = slice(k * NG + q * BANK, k * NG + (q + 1) * BANK)
                    m = nc.vector.tensor_tensor(lo[c][:, cols], raw[c][k % 2][:, q * BANK:(q + 1) * BANK],
                                                hi[c][:, cols].bitcast(F32), ALU.subtract)
                m.then_inc(w_lo_ready, 1)

            for m in range(NBANK):
                g, i0 = m // (NBANK // (CH * GROUPS)), m % (NBANK // (CH * GROUPS)) * BPAIRS
                c = g // GROUPS
                dve.wait_ge(conv_done, m + 1)
                if i0 == 0:
                    if g == 0:
                        dve.wait_ge(tap_rows_stored, 48)
                    else:
                        dve.wait_ge(xres_stored, 16 * g)
                ch = c * 2 * P + (g % GROUPS) * SLICE + i0
                bias = conv_bias[:, c * 2 * P:(c + 1) * 2 * P].rearrange("b (h i) -> b i h", h=2)
                i1 = (g % GROUPS) * SLICE + i0
                nc.vector.tensor_tensor(
                    stage[:, :].rearrange("b (u h i) -> b i h u", h=2, i=SLICE)[:, i0:i0 + BPAIRS],
                    bank[m % 8][:, :].rearrange("b (i h u) -> b i h u", i=BPAIRS, h=2),
                    bias[:, i1:i1 + BPAIRS, :].unsqueeze(3).to_broadcast([P, BPAIRS, 2, T]),
                    ALU.add,
                ).then_inc(stage_ready, 1)
                p, end = m // PBANKS, m % PBANKS == PBANKS - 1
                if p >= NPIECE - KB and end:
                    split_lo(0, p - (NPIECE - KB))

            for k in range(KB):
                split_lo(1, k)
            dve.wait_ge(gate_bias_loaded, 32)
            nc.vector.tensor_tensor(bias_rz[:, :], bias_ih[:, 0:N], bias_hh[:, 0:N],
                                    ALU.add).then_inc(bias_rz_ready, 1)
            dve.wait_ge(bias_rz_ready, 1)

            def low_part(lo_out, psum, hi_in, hi_ready, lo_ready, count):
                dve.wait_ge(hi_ready, count)
                nc.vector.tensor_tensor(lo_out[:, :], psum[:, :], hi_in[:, :].bitcast(F32),
                                        ALU.subtract).then_inc(lo_ready, 1)

            low_part(hT_lo, ps_hT, hT_hi, hT_hi_ready, hT_lo_ready, 1)
            low_part(xT_lo, ps_xT, xT_hi, xT_hi_ready, xT_lo_ready, 1)

            def step(i, u):
                t = i * RING + u
                dve.wait_ge(gi_done, t + 1)
                nc.vector.tensor_tensor(new_x[:, :], ps_in[:, :], bias_ih[:, N:NG], ALU.add).then_inc(new_x_ready, 1)
                dve.wait_ge(gh_r_done, t + 1)
                nc.vector.tensor_tensor(pre_r[:, :], ps_r[:, :], bias_rz[:, R:R + D], ALU.add).then_inc(pre_r_ready, 1)
                if not last(i, u):
                    low_part(xT_lo, ps_xT, xT_hi, xT_hi_ready, xT_lo_ready, t + 2)
                dve.wait_ge(gh_n_done, t + 1)
                nc.vector.tensor_tensor(new_h[:, :], ps_hn[:, :], bias_hh[:, N:NG], ALU.add).then_inc(new_h_ready, 1)
                dve.wait_ge(new_h_ready, t + 1)
                dve.wait_ge(r_ready, t + 1)
                nc.vector.tensor_tensor(reset_h[:, :], new_h[:, :], r[:, :], ALU.mult).then_inc(reset_h_ready, 1)
                dve.wait_ge(reset_h_ready, t + 1)
                nc.vector.tensor_tensor(pre_n[:, :], reset_h[:, :], new_x[:, :], ALU.add).then_inc(pre_n_ready, 1)
                dve.wait_ge(n_ready, t + 1)
                nc.vector.tensor_tensor(h_less_n[:, :], h[:, :], n_gate[:, :],
                                        ALU.subtract).then_inc(h_less_n_ready, 1)
                dve.wait_ge(gh_z_done, t + 1)
                nc.vector.tensor_tensor(pre_z[:, :], ps_z[:, :], bias_rz[:, Z:Z + D], ALU.add).then_inc(pre_z_ready, 1)
                dve.wait_ge(h_less_n_ready, t + 1)
                dve.wait_ge(z_ready, t + 1)
                nc.vector.tensor_tensor(z_part[:, :], z[:, :], h_less_n[:, :], ALU.mult).then_inc(z_part_ready, 1)
                dve.wait_ge(z_part_ready, t + 1)
                nc.vector.tensor_tensor(h[:, :], n_gate[:, :], z_part[:, :], ALU.add).then_inc(h_ready, 1)
                dve.wait_ge(h_ready, t + 1)
                if isinstance(i, bass.RuntimeValue) or i > 0:
                    dve.wait_ge(out_stored[u], 16 * i)
                for c in range(CH):
                    m = nc.vector.tensor_tensor(
                        out_t[u][:, c * 2 * P:(c + 1) * 2 * P].rearrange("b (h g i) -> b h g i", h=2, g=GROUPS),
                        xt[u][:, c * 2 * P:(c + 1) * 2 * P].rearrange("b (g h i) -> b h g i", h=2, g=GROUPS),
                        h[:, c * 2 * P:(c + 1) * 2 * P].rearrange("b (h g i) -> b h g i", h=2, g=GROUPS),
                        ALU.add)
                m.then_inc(out_ready, 1)
                if not last(i, u):
                    low_part(hT_lo, ps_hT, hT_hi, hT_hi_ready, hT_lo_ready, t + 2)

            dve.wait_ge(h0_loaded, 16)
            rounds(dve, True, step)

        @block.tensor
        def _(pe):
            for p in range(NPIECE):
                c, i0 = p // (NPIECE // CH), p % (NPIECE // CH) * PIECE
                if i0 == 0:
                    pe.wait_ge(x_loaded[c], 32)
                pe.wait_ge(diag_ready, p + 1)
                for j in range(PIECE):
                    m = (p * PIECE + j) // BPAIRS
                    if j % BPAIRS == 0 and m >= 8:
                        pe.wait_ge(stage_ready, m - 7)
                    mm = nc.tensor.matmul(
                        bank[m % 8][:, j % BPAIRS * P:(j % BPAIRS + 1) * P],
                        x_sb[c][:, :].rearrange("s (b i) -> s i b", b=B)[:, i0 + j, :],
                        diag[p % 2][:, j * P:(j + 1) * P], start=True, stop=True)
                    if j % BPAIRS == BPAIRS - 1:
                        mm.then_inc(conv_done, 1)

            def transpose(psum, done, block_of):
                for k in range(KB):
                    mm = nc.tensor.transpose(psum[:, k * P:(k + 1) * P], block_of(k), ident[:, :])
                mm.then_inc(done, 1)

            def h_block(k):
                return h[:, k * P:(k + 1) * P]

            def x_block(u):
                return lambda k: xt[u][:, k * P:(k + 1) * P]

            def product(psum, part_hi, part_lo, which, gate, start, stop):
                for k in range(KB):
                    rows = slice(k * P, (k + 1) * P)
                    cols = slice(k * NG + gate, k * NG + gate + D)
                    for n, (a, w) in enumerate(((part_hi, hi), (part_hi, lo), (part_lo, hi))):
                        mm = nc.tensor.matmul(psum[:, :], a[:, rows], w[which][:, cols],
                                              start=start and k == 0 and n == 0,
                                              stop=stop and k == KB - 1 and n == 2)
                return mm

            def x_product(psum, gate, stop):
                return product(psum, xT_hi, xT_lo, 0, gate, True, stop)

            def h_product(psum, gate, start):
                return product(psum, hT_hi, hT_lo, 1, gate, start, True)

            pe.wait_ge(ident_set, 2)
            pe.wait_ge(h0_loaded, 16)
            pe.wait_ge(stage_ready, NBANK)
            transpose(ps_hT, hT_done, h_block)
            pe.wait_ge(xt_loaded[0], 16)
            transpose(ps_xT, xT_done, x_block(0))
            pe.wait_ge(w_lo_ready, KB)
            pe.wait_ge(xT_lo_ready, 1)
            x_product(ps_r, R, False)
            x_product(ps_in, N, True)
            x_product(ps_z, Z, False).then_inc(gi_done, 1)
            pe.wait_ge(w_lo_ready, 2 * KB)

            def step(i, u):
                t = i * RING + u
                pe.wait_ge(hT_lo_ready, t + 1)
                h_product(ps_r, R, False).then_inc(gh_r_done, 1)
                if not last(i, u):
                    nxt = (u + 1) % RING
                    pe.wait_ge(xt_loaded[nxt], 16 * (i + (u + 1) // RING) + 16)
                    transpose(ps_xT, xT_done, x_block(nxt))
                h_product(ps_hn, N, True).then_inc(gh_n_done, 1)
                h_product(ps_z, Z, False).then_inc(gh_z_done, 1)
                if not last(i, u):
                    pe.wait_ge(xT_lo_ready, t + 2)
                    pe.wait_ge(pre_r_ready, t + 1)
                    x_product(ps_r, R, False)
                    pe.wait_ge(new_x_ready, t + 1)
                    x_product(ps_in, N, True)
                    pe.wait_ge(h_ready, t + 1)
                    transpose(ps_hT, hT_done, h_block)
                    pe.wait_ge(pre_z_ready, t + 1)
                    x_product(ps_z, Z, False).then_inc(gi_done, 1)

            rounds(pe, False, step)


_INS = ["x", "cond_2048", "L0_cond_b", "L1_cond_W_ih", "L1_cond_W_hh", "L1_cond_b_ih", "L1_cond_b_hh"]
_OUTS = [((128, 64, 512), "float32")]


def kernel(**inputs):
    import numpy as _np
    import concourse.bacc as _bacc
    from concourse import mybir as _mybir
    from concourse.bass_utils import run_bass_kernel_spmd as _run

    nc = _bacc.Bacc("TRN2", target_bir_lowering=False, num_devices=1, dynamic_dma_scratch_size=1024)
    arrays, args = {}, []
    for name in _INS:
        a = _np.ascontiguousarray(inputs[name])
        arrays[f"in_{name}_dram"] = a
        args.append(nc.dram_tensor(f"in_{name}_dram", a.shape, _mybir.dt.from_np(a.dtype), kind="ExternalInput").ap())
    for i, (shape, dtype) in enumerate(_OUTS):
        dt = _mybir.dt.from_np(_np.dtype(dtype))
        args.append(nc.dram_tensor(f"out_{i}_dram", shape, dt, kind="ExternalOutput").ap())
    conv_residual_gru(nc, *args)
    r = _run(nc, [arrays], core_ids=[0])
    return r.results[0]["out_0_dram"]
```

```python
from contextlib import ExitStack

import concourse.bass as bass
from concourse import mybir

P = 128
F32 = mybir.dt.float32
F32R = mybir.dt.float32r
ALU = mybir.AluOpType
ACT = mybir.ActivationFunctionType

KW = 4
RING = 4
SLICE = 32
PIECE = 8
BANK = 512


def conv_residual_gru(
    nc: bass.Bass,
    x: bass.AP,
    taps: bass.AP,
    conv_b: bass.AP,
    w_ih: bass.AP,
    w_hh: bass.AP,
    b_ih: bass.AP,
    b_hh: bass.AP,
    out: bass.AP,
):
    B, T, D = x.shape
    K = taps.shape[0]
    NG = w_ih.shape[1]
    assert B == P and 2 * T == P and NG == 3 * D and D == 4 * P == BANK and K >= T and taps.shape[1] == D
    KB = D // P
    CH = D // (2 * P)
    GROUPS = P // SLICE
    PIECES = SLICE // PIECE
    NPIECE = CH * GROUPS * PIECES
    BPAIRS = BANK // P
    NBANK = CH * P // BPAIRS
    PBANKS = PIECE // BPAIRS
    STRIPS = P // SLICE

    def x_strip(k, q):
        c, g = k // 2, k % 2 * 2 + q // 2
        return c * 2 * P + q % 2 * P + g * SLICE

    R, Z, N = 0, D, 2 * D

    CHUNK_BANKS, GROUP_BANKS = NBANK // CH, NBANK // (CH * GROUPS)
    HALF_U = T // 2
    GCOLS = T * 2 * SLICE

    tap_rows = nc.dram_tensor("tap_rows", [2 * T, D], F32, kind="Internal").ap()
    xres = nc.dram_tensor("xres", [GROUPS, B, T, 2 * SLICE], F32, kind="Internal").ap()

    top = [2048]

    def place(name, cols, dtype=F32, parts=P):
        t = nc.alloc_sbuf_tensor_at(name, [parts, cols], dtype, offset=top[0])
        top[0] += cols * KW
        return t

    x0_at = top[0]
    x_sb = [place(f"x_sb{c}", B * P) for c in range(CH)]
    x1_at = x0_at + B * P * KW
    toep1_at = top[0]
    toep1 = place("toep1", T * P)
    diag_at = top[0]
    diag = [place(f"diag{n}", PIECE * P) for n in range(2)]
    conv_bias = place("conv_bias", D)
    ident = place("ident", P)
    h = place("h", D)
    toep0_at = top[0]
    toep0 = place("toep0", T * P)
    toep = [toep0, toep1]
    stage_at = top[0]
    stage_odd = place("stage_odd", GCOLS)
    assert top[0] <= nc.SBUF_PARTITION_SIZE_BYTES - 64

    top[0] = toep1_at + HALF_U * P * KW
    stage_even = place("stage_even", GCOLS)
    assert top[0] <= diag_at
    top[0] = x0_at
    kept = place("kept", GROUPS * GCOLS)
    assert top[0] <= x1_at
    top[0] = stage_at
    lag0 = place("lag0", D, parts=1)
    zeros = place("zeros", D, parts=T)

    top[0] = toep0_at
    raw = [place(f"w_{name}_raw", KB * NG) for name in ("ih", "hh")]
    assert top[0] <= stage_at + GCOLS * KW
    top[0] = x1_at
    hi, lo = [], []
    for name in ("ih", "hh"):
        hi.append(place(f"w_{name}_hi", KB * NG, F32R))
        lo.append(place(f"w_{name}_lo", KB * NG, F32R))
    assert top[0] <= diag_at

    top[0] = diag_at
    hT_hi, hT_lo, xT_hi, xT_lo = (place(n, D, F32R) for n in ("hT_hi", "hT_lo", "xT_hi", "xT_lo"))
    xt = [place("xt0", D)]
    assert top[0] <= diag_at + (2 * PIECE * P + D) * KW
    top[0] = toep0_at
    xt += [place(f"xt{n}", D) for n in range(1, RING)]
    out_t = [place(f"out_t{n}", D) for n in range(RING)]
    pre_r, pre_z, r, z, n_gate = (place(n, D) for n in ("pre_r", "pre_z", "r", "z", "n_gate"))
    new_h, new_x, reset_h, pre_n = (place(n, D) for n in ("new_h", "new_x", "reset_h", "pre_n"))
    h_less_n = place("h_less_n", D)
    bias_ih, bias_hh = place("bias_ih", NG), place("bias_hh", NG)
    assert top[0] <= stage_at + GCOLS * KW

    def stage(g):
        if g >= GROUPS:
            return kept[:, (g - GROUPS) * GCOLS:(g - GROUPS + 1) * GCOLS]
        return (stage_odd if g % 2 else stage_even)[:, :]

    ctx = ExitStack()
    with ctx:
        bank = [ctx.enter_context(nc.psum_tensor(f"bank{n}", [P, BANK], F32)) for n in range(8)]
        ps_r, ps_z, ps_in, ps_hn, ps_xT, ps_hT = bank[:6]

        def sem(name):
            return ctx.enter_context(nc.semaphore(name))

        lag0_loaded = sem("lag0_loaded")
        lag0_plus_one = sem("lag0_plus_one")
        zeros_set = sem("zeros_set")
        tap_rows_stored = sem("tap_rows_stored")
        x_loaded = [sem(f"x_loaded{c}") for c in range(CH)]
        toep_loaded = [sem(f"toep_loaded{c}") for c in range(CH)]
        bias_loaded = sem("bias_loaded")
        diag_zeroed = sem("diag_zeroed")
        ident_set = sem("ident_set")
        diag_ready = sem("diag_ready")
        conv_done = sem("conv_done")
        stage_ready = sem("stage_ready")
        xres_stored = [sem(f"xres_stored{n}") for n in ("_even", "_odd")]
        toep_zeroed = [sem(f"toep_zeroed{n}") for n in range(2)]
        raw_loaded = [sem(f"raw_loaded_{name}") for name in ("ih", "hh")]
        w_hi_ready = sem("w_hi_ready")
        w_lo_ready = sem("w_lo_ready")
        h0_loaded = sem("h0_loaded")
        gate_bias_loaded = sem("gate_bias_loaded")
        bias_rz_ready = sem("bias_rz_ready")
        xt_loaded = [sem(f"xt_loaded{n}") for n in range(RING)]
        xT_done = sem("xT_done")
        xT_hi_ready = sem("xT_hi_ready")
        xT_lo_ready = sem("xT_lo_ready")
        hT_done = sem("hT_done")
        hT_hi_ready = sem("hT_hi_ready")
        hT_lo_ready = sem("hT_lo_ready")
        gi_done = sem("gi_done")
        gh_r_done = sem("gh_r_done")
        gh_n_done = sem("gh_n_done")
        gh_z_done = sem("gh_z_done")
        new_x_ready = sem("new_x_ready")
        pre_r_ready = sem("pre_r_ready")
        r_ready = sem("r_ready")
        new_h_ready = sem("new_h_ready")
        reset_h_ready = sem("reset_h_ready")
        pre_n_ready = sem("pre_n_ready")
        n_ready = sem("n_ready")
        h_less_n_ready = sem("h_less_n_ready")
        pre_z_ready = sem("pre_z_ready")
        z_ready = sem("z_ready")
        z_part_ready = sem("z_part_ready")
        h_ready = sem("h_ready")
        out_ready = sem("out_ready")
        out_stored = [sem(f"out_stored{n}") for n in range(RING)]

        ROUNDS = T // RING
        assert T % RING == 0 and ROUNDS >= 3

        def rounds(eng, first, body):
            if first:
                for u in range(RING):
                    body(0, u)
            with eng.Fori(1 if first else 0, ROUNDS - 1) as i:
                for u in range(RING):
                    body(i, u)
            for u in range(RING):
                body(ROUNDS - 1, u)

        def last(i, u):
            return not isinstance(i, bass.RuntimeValue) and i == ROUNDS - 1 and u == RING - 1

        def thirds(k):
            return [slice(c, c + D) for c in range(k * NG, (k + 1) * NG, D)]

        block = ctx.enter_context(nc.Block())

        def load_toeplitz(eng, c, part):
            for half in range(2):
                ch = (2 * c + half) * P
                rows = T - part * HALF_U
                src = tap_rows[part * HALF_U:, ch:ch + P]
                src = bass.AP(src.tensor, src.offset, [[D, rows], [D, HALF_U], [1, P]])
                cols = slice(part * HALF_U * P, (part + 1) * HALF_U * P)
                eng.dma_start(toep[c][half * T:half * T + rows, cols].rearrange("s (u i) -> s u i", i=P),
                              src).then_inc(toep_loaded[c], 16)

        def zero_toeplitz(eng, c, half):
            eng.memset(toep[c][half * T + HALF_U:(half + 1) * T, HALF_U * P:T * P], 0.0).then_inc(toep_zeroed[half], 1)

        @block.sync
        def _(sp):
            def load_x(c, b0, b1):
                for half in range(2):
                    ch = (2 * c + half) * P
                    sp.dma_start(
                        x_sb[c][half * T:(half + 1) * T, b0 * P:b1 * P].rearrange("s (b i) -> s b i", i=P),
                        x[b0:b1, :, ch:ch + P].rearrange("b s i -> s b i"),
                    ).then_inc(x_loaded[c], 16)

            def store_group(g):
                sp.wait_ge(stage_ready, (g + 1) * GROUP_BANKS)
                sp.dma_start(xres[g].rearrange("b u e -> b (u e)"), stage(g)).then_inc(xres_stored[g % 2], 16)

            load_x(0, 0, B)
            sp.wait_ge(toep_loaded[0], 64)
            load_x(1, 0, B // 2)
            store_group(0)
            load_x(1, B // 2, B)
            store_group(1)
            load_toeplitz(sp, 1, 0)
            store_group(2)
            sp.wait_ge(xres_stored[0], 32)
            load_toeplitz(sp, 1, 1)
            store_group(3)

            sp.wait_ge(diag_ready, NPIECE // CH)
            sp.wait_ge(xres_stored[1], 32)
            for which, w in enumerate((w_ih, w_hh)):
                for k in range(KB):
                    for q in range(STRIPS):
                        row = k * P + q * SLICE if which else x_strip(k, q)
                        sp.dma_start(raw[which][q * SLICE:(q + 1) * SLICE, k * NG:(k + 1) * NG],
                                     w[row:row + SLICE, :]).then_inc(raw_loaded[which], 16)

            def load_xt(u, back):
                sp.dma_start(
                    xt[u][:, 0:D // 2].rearrange("b (g o e) -> b g o e", g=GROUPS, o=1),
                    xres[:, :, bass.ds(back, 1), :].rearrange("g b o e -> b g o e"),
                ).then_inc(xt_loaded[u], 16)
                sp.dma_start(
                    xt[u][:, D // 2:D].rearrange("b (g e) -> b g e", g=GROUPS),
                    kept[:, :].rearrange("b (g u e) -> b g (u e)", g=GROUPS, u=T)[
                        :, :, bass.ds(back * (2 * SLICE), 2 * SLICE)],
                ).then_inc(xt_loaded[u], 16)

            sp.wait_ge(stage_ready, NBANK)
            load_xt(0, T - 1)
            sp.wait_ge(w_lo_ready, 2 * KB)
            for b, bias in ((b_ih, bias_ih), (b_hh, bias_hh)):
                sp.dma_start(bias[:, :], b.partition_broadcast(P)).then_inc(gate_bias_loaded, 16)
            for t in range(1, RING):
                load_xt(t, T - 1 - t)

            def step(i, u):
                sp.wait_ge(out_ready, i * RING + u + 1)
                t = i * RING + u
                sp.dma_start(out[:, bass.ds(t, 1), :].rearrange("b o d -> b (o d)"),
                             out_t[u][:, :]).then_inc(out_stored[u], 16)
                if isinstance(i, bass.RuntimeValue) or i < ROUNDS - 1:
                    load_xt(u, T - 1 - RING - u - i * RING)

            rounds(sp, False, step)
            for u in range(RING):
                sp.wait_ge(out_stored[u], 16 * ROUNDS)

        @block.gpsimd
        def _(pool):
            nc.gpsimd.memset(zeros[:, :], 0.0).then_inc(zeros_set, 1)
            for n in range(2):
                nc.gpsimd.memset(diag[n][:, :], 0.0).then_inc(diag_zeroed, 1)
            nc.gpsimd.memset(ident[:, :], 0.0).then_inc(ident_set, 1)
            pool.wait_ge(ident_set, 1)
            nc.gpsimd.affine_select(out=ident[:, :], in_=ident[:, :], compare_op=ALU.not_equal, fill=1.0,
                                    base=0, pattern=[[-1, P]], channel_multiplier=1).then_inc(ident_set, 1)
            pool.wait_ge(ident_set, 2)
            zero_toeplitz(nc.gpsimd, 0, 0)
            pool.wait_ge(toep_zeroed[0], 1)
            pool.wait_ge(xres_stored[0], 32)
            zero_toeplitz(nc.gpsimd, 1, 0)

        @block.scalar
        def _(act):
            act.dma_start(lag0[:, :], taps[K - 1:K, :]).then_inc(lag0_loaded, 16)
            act.dma_start(conv_bias[:, :], conv_b.partition_broadcast(P)).then_inc(bias_loaded, 16)
            act.dma_start(tap_rows[0:T - 1, :], taps[K - T:K - 1, :]).then_inc(tap_rows_stored, 16)
            act.dma_start(h[:, :], taps).then_inc(h0_loaded, 16)
            act.wait_ge(zeros_set, 1)
            act.dma_start(tap_rows[T:2 * T, :], zeros[:, :]).then_inc(tap_rows_stored, 16)
            act.wait_ge(lag0_plus_one, 1)
            act.dma_start(tap_rows[T - 1:T, :], lag0[:, :]).then_inc(tap_rows_stored, 16)
            act.wait_ge(tap_rows_stored, 48)
            for part in range(2):
                load_toeplitz(act, 0, part)

            act.wait_ge(diag_zeroed, 2)
            for p in range(NPIECE):
                c, i0 = p // (NPIECE // CH), p % (NPIECE // CH) * PIECE
                if i0 == 0:
                    act.wait_ge(toep_loaded[c], 64)
                    for half in range(2):
                        act.wait_ge(toep_zeroed[half], c + 1)
                if p >= 2:
                    act.wait_ge(conv_done, (p - 1) * PBANKS)
                for half in range(2):
                    rows = slice(half * T, (half + 1) * T)
                    m = nc.scalar.activation(
                        diag[p % 2][rows, :].rearrange("s (i h u) -> s i h u", i=PIECE, h=2)[:, :, half, :],
                        toep[c][rows, :].rearrange("s (u i) -> s i u", u=T)[:, i0:i0 + PIECE, :], ACT.Copy)
                m.then_inc(diag_ready, 1)

            act.wait_ge(conv_done, NBANK)
            for which in range(2):
                act.wait_ge(raw_loaded[which], 16 * KB * STRIPS)
                for k in range(KB):
                    for cols in thirds(k):
                        m = nc.scalar.activation(hi[which][:, cols], raw[which][:, cols], ACT.Copy)
                        m.then_inc(w_hi_ready, 1)
                if which == 0:
                    act.wait_ge(hT_done, 1)
                    nc.scalar.activation(hT_hi[:, :], ps_hT[:, :], ACT.Copy).then_inc(hT_hi_ready, 1)
                    act.wait_ge(xT_done, 1)
                    nc.scalar.activation(xT_hi[:, :], ps_xT[:, :], ACT.Copy).then_inc(xT_hi_ready, 1)

            def step(i, u):
                t = i * RING + u
                act.wait_ge(pre_r_ready, t + 1)
                nc.scalar.activation(r[:, :], pre_r[:, :], ACT.Sigmoid).then_inc(r_ready, 1)
                if not last(i, u):
                    act.wait_ge(xT_done, t + 2)
                    nc.scalar.activation(xT_hi[:, :], ps_xT[:, :], ACT.Copy).then_inc(xT_hi_ready, 1)
                act.wait_ge(pre_n_ready, t + 1)
                nc.scalar.activation(n_gate[:, :], pre_n[:, :], ACT.Tanh).then_inc(n_ready, 1)
                act.wait_ge(pre_z_ready, t + 1)
                nc.scalar.activation(z[:, :], pre_z[:, :], ACT.Sigmoid).then_inc(z_ready, 1)
                if not last(i, u):
                    act.wait_ge(hT_done, t + 2)
                    nc.scalar.activation(hT_hi[:, :], ps_hT[:, :], ACT.Copy).then_inc(hT_hi_ready, 1)

            rounds(act, False, step)

        @block.vector
        def _(dve):
            dve.wait_ge(lag0_loaded, 16)
            nc.vector.tensor_scalar_add(lag0[:, :], lag0[:, :], 1.0).then_inc(lag0_plus_one, 1)
            dve.wait_ge(bias_loaded, 16)

            zero_toeplitz(nc.vector, 0, 1)

            def low_part(lo_out, psum, hi_in, hi_ready, lo_ready, count):
                dve.wait_ge(hi_ready, count)
                nc.vector.tensor_tensor(lo_out[:, :], psum[:, :], hi_in[:, :].bitcast(F32),
                                        ALU.subtract).then_inc(lo_ready, 1)

            for m in range(NBANK):
                g, i0 = m // GROUP_BANKS, m % GROUP_BANKS * BPAIRS
                c = g // GROUPS
                if m == CHUNK_BANKS:
                    dve.wait_ge(xres_stored[0], 32)
                    zero_toeplitz(nc.vector, 1, 1)
                dve.wait_ge(conv_done, m + 1)
                if i0 == 0 and g == 1:
                    dve.wait_ge(tap_rows_stored, 48)
                elif i0 == 0 and g in (2, 3):
                    dve.wait_ge(xres_stored[g % 2], 16)
                i1 = (g % GROUPS) * SLICE + i0
                bias = conv_bias[:, c * 2 * P:(c + 1) * 2 * P].rearrange("b (h i) -> b i h", h=2)
                nc.vector.tensor_tensor(
                    stage(g).rearrange("b (u h i) -> b i h u", h=2, i=SLICE)[:, i0:i0 + BPAIRS],
                    bank[m % 8][:, :].rearrange("b (i h u) -> b i h u", i=BPAIRS, h=2),
                    bias[:, i1:i1 + BPAIRS, :].unsqueeze(3).to_broadcast([P, BPAIRS, 2, T]),
                    ALU.add,
                ).then_inc(stage_ready, 1)

            for which in range(2):
                for k in range(KB):
                    for n, cols in enumerate(thirds(k)):
                        dve.wait_ge(w_hi_ready, (which * KB + k) * 3 + n + 1)
                        m = nc.vector.tensor_tensor(lo[which][:, cols], raw[which][:, cols],
                                                    hi[which][:, cols].bitcast(F32), ALU.subtract)
                    m.then_inc(w_lo_ready, 1)

                if which == 0:
                    low_part(hT_lo, ps_hT, hT_hi, hT_hi_ready, hT_lo_ready, 1)
                    low_part(xT_lo, ps_xT, xT_hi, xT_hi_ready, xT_lo_ready, 1)

            dve.wait_ge(gate_bias_loaded, 32)
            nc.vector.tensor_tensor(bias_ih[:, 0:N], bias_ih[:, 0:N], bias_hh[:, 0:N],
                                    ALU.add).then_inc(bias_rz_ready, 1)
            dve.wait_ge(bias_rz_ready, 1)

            def step(i, u):
                t = i * RING + u
                dve.wait_ge(gi_done, t + 1)
                nc.vector.tensor_tensor(new_x[:, :], ps_in[:, :], bias_ih[:, N:NG], ALU.add).then_inc(new_x_ready, 1)
                dve.wait_ge(gh_r_done, t + 1)
                nc.vector.tensor_tensor(pre_r[:, :], ps_r[:, :], bias_ih[:, R:R + D], ALU.add).then_inc(pre_r_ready, 1)
                if not last(i, u):
                    low_part(xT_lo, ps_xT, xT_hi, xT_hi_ready, xT_lo_ready, t + 2)
                dve.wait_ge(gh_n_done, t + 1)
                nc.vector.tensor_tensor(new_h[:, :], ps_hn[:, :], bias_hh[:, N:NG], ALU.add).then_inc(new_h_ready, 1)
                dve.wait_ge(new_h_ready, t + 1)
                dve.wait_ge(r_ready, t + 1)
                nc.vector.tensor_tensor(reset_h[:, :], new_h[:, :], r[:, :], ALU.mult).then_inc(reset_h_ready, 1)
                dve.wait_ge(reset_h_ready, t + 1)
                nc.vector.tensor_tensor(pre_n[:, :], reset_h[:, :], new_x[:, :], ALU.add).then_inc(pre_n_ready, 1)
                dve.wait_ge(n_ready, t + 1)
                nc.vector.tensor_tensor(h_less_n[:, :], h[:, :], n_gate[:, :],
                                        ALU.subtract).then_inc(h_less_n_ready, 1)
                dve.wait_ge(gh_z_done, t + 1)
                nc.vector.tensor_tensor(pre_z[:, :], ps_z[:, :], bias_ih[:, Z:Z + D], ALU.add).then_inc(pre_z_ready, 1)
                dve.wait_ge(h_less_n_ready, t + 1)
                dve.wait_ge(z_ready, t + 1)
                nc.vector.tensor_tensor(h_less_n[:, :], z[:, :], h_less_n[:, :], ALU.mult).then_inc(z_part_ready, 1)
                dve.wait_ge(z_part_ready, t + 1)
                nc.vector.tensor_tensor(h[:, :], n_gate[:, :], h_less_n[:, :], ALU.add).then_inc(h_ready, 1)
                dve.wait_ge(h_ready, t + 1)
                if isinstance(i, bass.RuntimeValue) or i > 0:
                    dve.wait_ge(out_stored[u], 16 * i)
                for c in range(CH):
                    m = nc.vector.tensor_tensor(
                        out_t[u][:, c * 2 * P:(c + 1) * 2 * P].rearrange("b (h g i) -> b h g i", h=2, g=GROUPS),
                        xt[u][:, c * 2 * P:(c + 1) * 2 * P].rearrange("b (g h i) -> b h g i", h=2, g=GROUPS),
                        h[:, c * 2 * P:(c + 1) * 2 * P].rearrange("b (h g i) -> b h g i", h=2, g=GROUPS),
                        ALU.add)
                m.then_inc(out_ready, 1)
                if not last(i, u):
                    low_part(hT_lo, ps_hT, hT_hi, hT_hi_ready, hT_lo_ready, t + 2)

            dve.wait_ge(h0_loaded, 16)
            rounds(dve, True, step)

        @block.tensor
        def _(pe):
            for p in range(NPIECE):
                c, i0 = p // (NPIECE // CH), p % (NPIECE // CH) * PIECE
                if i0 == 0:
                    pe.wait_ge(x_loaded[c], 64 if c else 32)
                pe.wait_ge(diag_ready, p + 1)
                for j in range(PIECE):
                    m = (p * PIECE + j) // BPAIRS
                    if j % BPAIRS == 0 and m >= 8:
                        pe.wait_ge(stage_ready, m - 7)
                    mm = nc.tensor.matmul(
                        bank[m % 8][:, j % BPAIRS * P:(j % BPAIRS + 1) * P],
                        x_sb[c][:, :].rearrange("s (b i) -> s i b", b=B)[:, i0 + j, :],
                        diag[p % 2][:, j * P:(j + 1) * P], start=True, stop=True)
                    if j % BPAIRS == BPAIRS - 1:
                        mm.then_inc(conv_done, 1)

            def transpose(psum, done, block_of):
                for k in range(KB):
                    mm = nc.tensor.transpose(psum[:, k * P:(k + 1) * P], block_of(k), ident[:, :])
                mm.then_inc(done, 1)

            def h_block(k):
                return h[:, k * P:(k + 1) * P]

            def x_block(u):
                return lambda k: xt[u][:, k * P:(k + 1) * P]

            def product(psum, part_hi, part_lo, which, gate, start, stop):
                for k in range(KB):
                    rows = slice(k * P, (k + 1) * P)
                    cols = slice(k * NG + gate, k * NG + gate + D)
                    for n, (a, w) in enumerate(((part_hi, hi), (part_hi, lo), (part_lo, hi))):
                        mm = nc.tensor.matmul(psum[:, :], a[:, rows], w[which][:, cols],
                                              start=start and k == 0 and n == 0,
                                              stop=stop and k == KB - 1 and n == 2)
                return mm

            def x_product(psum, gate, stop):
                return product(psum, xT_hi, xT_lo, 0, gate, True, stop)

            def h_product(psum, gate, start):
                return product(psum, hT_hi, hT_lo, 1, gate, start, True)

            pe.wait_ge(ident_set, 2)
            pe.wait_ge(h0_loaded, 16)
            pe.wait_ge(stage_ready, NBANK)
            transpose(ps_hT, hT_done, h_block)
            pe.wait_ge(xt_loaded[0], 32)
            transpose(ps_xT, xT_done, x_block(0))
            pe.wait_ge(w_lo_ready, KB)
            pe.wait_ge(xT_lo_ready, 1)
            x_product(ps_r, R, False)
            x_product(ps_in, N, True)
            x_product(ps_z, Z, False).then_inc(gi_done, 1)
            pe.wait_ge(w_lo_ready, 2 * KB)

            def step(i, u):
                t = i * RING + u
                pe.wait_ge(hT_lo_ready, t + 1)
                h_product(ps_r, R, False).then_inc(gh_r_done, 1)
                if not last(i, u):
                    nxt = (u + 1) % RING
                    pe.wait_ge(xt_loaded[nxt], 32 * (i + (u + 1) // RING) + 32)
                    transpose(ps_xT, xT_done, x_block(nxt))
                h_product(ps_hn, N, True).then_inc(gh_n_done, 1)
                h_product(ps_z, Z, False).then_inc(gh_z_done, 1)
                if not last(i, u):
                    pe.wait_ge(xT_lo_ready, t + 2)
                    pe.wait_ge(pre_r_ready, t + 1)
                    x_product(ps_r, R, False)
                    pe.wait_ge(new_x_ready, t + 1)
                    x_product(ps_in, N, True)
                    pe.wait_ge(h_ready, t + 1)
                    transpose(ps_hT, hT_done, h_block)
                    pe.wait_ge(pre_z_ready, t + 1)
                    x_product(ps_z, Z, False).then_inc(gi_done, 1)

            rounds(pe, False, step)


_INS = ["x", "cond_2048", "L0_cond_b", "L1_cond_W_ih", "L1_cond_W_hh", "L1_cond_b_ih", "L1_cond_b_hh"]
_OUTS = [((128, 64, 512), "float32")]


def kernel(**inputs):
    import numpy as _np
    import concourse.bacc as _bacc
    from concourse import mybir as _mybir
    from concourse.bass_utils import run_bass_kernel_spmd as _run

    nc = _bacc.Bacc("TRN2", target_bir_lowering=False, num_devices=1, dynamic_dma_scratch_size=1024)
    arrays, args = {}, []
    for name in _INS:
        a = _np.ascontiguousarray(inputs[name])
        arrays[f"in_{name}_dram"] = a
        args.append(nc.dram_tensor(f"in_{name}_dram", a.shape, _mybir.dt.from_np(a.dtype), kind="ExternalInput").ap())
    for i, (shape, dtype) in enumerate(_OUTS):
        dt = _mybir.dt.from_np(_np.dtype(dtype))
        args.append(nc.dram_tensor(f"out_{i}_dram", shape, dt, kind="ExternalOutput").ap())
    conv_residual_gru(nc, *args)
    r = _run(nc, [arrays], core_ids=[0])
    return r.results[0]["out_0_dram"]
```

```python
from contextlib import ExitStack

import concourse.bass as bass
from concourse import mybir

P = 128
F32 = mybir.dt.float32
F32R = mybir.dt.float32r
ALU = mybir.AluOpType
ACT = mybir.ActivationFunctionType

KW = 4
RING = 4
SLICE = 32
PIECE = 8
BANK = 512


def conv_residual_gru(
    nc: bass.Bass,
    x: bass.AP,
    taps: bass.AP,
    conv_b: bass.AP,
    w_ih: bass.AP,
    w_hh: bass.AP,
    b_ih: bass.AP,
    b_hh: bass.AP,
    out: bass.AP,
):
    B, T, D = x.shape
    K = taps.shape[0]
    NG = w_ih.shape[1]
    assert B == P and 2 * T == P and NG == 3 * D and D == 4 * P == BANK and K >= T and taps.shape[1] == D
    KB = D // P
    CH = D // (2 * P)
    GROUPS = P // SLICE
    PIECES = SLICE // PIECE
    NPIECE = CH * GROUPS * PIECES
    QUADS = P // SLICE
    BPAIRS = BANK // P
    NBANK = CH * P // BPAIRS
    PBANKS = PIECE // BPAIRS

    def first_channel(k, q):
        c, g = k // 2, k % 2 * 2 + q // 2
        return c * 2 * P + q % 2 * P + g * SLICE

    R, Z, N = 0, D, 2 * D

    GROUP_BANKS = NBANK // (CH * GROUPS)
    GCOLS = T * 2 * SLICE

    xres = nc.dram_tensor("xres", [2, KB, B, T, 2 * SLICE], F32, kind="Internal").ap()

    top = [2048]

    def place(name, cols, dtype=F32):
        t = nc.alloc_sbuf_tensor_at(name, [P, cols], dtype, offset=top[0])
        top[0] += cols * KW
        return t

    x0_at = top[0]
    x_sb = [place(f"x_sb{c}", B * P) for c in range(CH)]
    x1_at = x0_at + B * P * KW
    toep1_at = top[0]
    top[0] += T * P * KW
    diag_at = top[0]
    diag = [place(f"diag{n}", PIECE * P) for n in range(2)]
    conv_bias = place("conv_bias", D)
    ident = place("ident", P + T)
    window_at = top[0]
    window = place("window", P + T, F32R)
    in_matrix = place("in_matrix", T)
    taps_at = top[0]
    taps_hi, taps_lo = (place(n, CH * P, F32R) for n in ("taps_hi", "taps_lo"))
    toep0_at = top[0]
    top[0] = toep1_at
    toep_span = place("toep_span", (toep0_at - toep1_at) // KW + T * P)
    to_toep0 = (toep0_at - toep1_at) // KW
    toep = [toep_span[:, to_toep0:to_toep0 + T * P], toep_span[:, 0:T * P]]
    stage_at = top[0]
    stages = [place("stage0", GCOLS)]
    assert top[0] <= nc.SBUF_PARTITION_SIZE_BYTES - 64

    QUARTER = B // 4
    assert QUARTER * P == GCOLS
    top[0] = x1_at + 3 * GCOLS * KW
    stages.append(place("stage1", GCOLS))
    assert top[0] == toep1_at
    top[0] = toep0_at
    stages.append(place("stage2", GCOLS))
    assert T * P // 2 == GCOLS and GROUPS == 4
    top[0] = x0_at
    kept = place("kept", GROUPS * GCOLS)
    top[0] = x0_at + (GROUPS - 1) * GCOLS * KW
    stages.append(place("stage3", GCOLS))
    assert top[0] <= x1_at
    top[0] = stage_at
    taps_sb = place("taps_sb", CH * P)
    taps_plus = place("taps_plus", CH * P)
    lag0_row = place("lag0_row", 1)
    top[0] = taps_at
    h = place("h", D)
    assert top[0] <= toep0_at
    top[0] = window_at
    x0_stored = place("x0_stored", D // 2)
    assert top[0] <= taps_at

    top[0] = toep0_at
    raw = [place(f"w_{name}_raw", KB * NG) for name in ("ih", "hh")]
    assert top[0] <= stage_at + GCOLS * KW
    top[0] = x1_at
    hi, lo = [], []
    for name in ("ih", "hh"):
        hi.append(place(f"w_{name}_hi", KB * NG, F32R))
        lo.append(place(f"w_{name}_lo", KB * NG, F32R))
    assert top[0] <= diag_at

    top[0] = diag_at
    hT_hi, hT_lo, xT_hi, xT_lo = (place(n, D, F32R) for n in ("hT_hi", "hT_lo", "xT_hi", "xT_lo"))
    x0_kept = place("x0_kept", D // 2)
    assert top[0] <= diag_at + (2 * PIECE * P + D) * KW
    top[0] = toep0_at
    bias_ih, bias_hh, bias_rz = place("bias_ih", NG), place("bias_hh", NG), place("bias_rz", N)
    xT = place("xT", D)
    x_quads1, x_quads2, xt0 = place("x_quads1", D), place("x_quads2", D), place("xt0", D)
    assert top[0] <= toep0_at + KB * NG * KW
    out_t0, out_t1 = place("out_t0", D), place("out_t1", D)
    pre_r, pre_z, r, z, n_gate = (place(n, D) for n in ("pre_r", "pre_z", "r", "z", "n_gate"))
    new_h, new_x, reset_h, pre_n = (place(n, D) for n in ("new_h", "new_x", "reset_h", "pre_n"))
    h_less_n = place("h_less_n", D)
    assert top[0] <= stage_at + GCOLS * KW
    top[0] = x0_at
    xt1, xt2, xt3 = (place(f"xt{n}", D) for n in (1, 2, 3))
    x_quads0, x_quads3 = place("x_quads0", D), place("x_quads3", D)
    out_t2, out_t3 = place("out_t2", D), place("out_t3", D)
    assert top[0] <= x0_at + GCOLS * KW
    xt = [xt0, xt1, xt2, xt3]
    x_quads = [x_quads0, x_quads1, x_quads2, x_quads3]
    out_t = [out_t0, out_t1, out_t2, out_t3]

    def stage(g):
        if g >= GROUPS:
            return kept[:, (g - GROUPS) * GCOLS:(g - GROUPS + 1) * GCOLS]
        return stages[g][:, :]

    ctx = ExitStack()
    with ctx:
        bank = [ctx.enter_context(nc.psum_tensor(f"bank{n}", [P, BANK], F32)) for n in range(8)]
        ps_r, ps_z, ps_in, ps_hn, ps_x0_first, ps_hT = bank[:6]
        ps_x0 = (ps_x0_first, ps_hn)

        def sem(name):
            return ctx.enter_context(nc.semaphore(name))

        taps_loaded = sem("taps_loaded")
        lag0_row_set = sem("lag0_row_set")
        taps_plus_ready = sem("taps_plus_ready")
        taps_hi_ready = sem("taps_hi_ready")
        taps_lo_ready = sem("taps_lo_ready")
        window_ready = sem("window_ready")
        in_matrix_set = sem("in_matrix_set")
        x_loaded = [sem(f"x_loaded{c}") for c in range(CH)]
        shift_done = sem("shift_done")
        toep_even_ready = sem("toep_even_ready")
        toep_odd_ready = sem("toep_odd_ready")
        bias_loaded = sem("bias_loaded")
        diag_zeroed = sem("diag_zeroed")
        ident_set = sem("ident_set")
        diag_ready = sem("diag_ready")
        conv_done = sem("conv_done")
        stage_ready = sem("stage_ready")
        xres_stored = [sem(f"xres_stored{g}") for g in range(CH * GROUPS)]
        group0_stored = [sem(f"group0_stored{n}") for n in range(2)]
        group1_stored = [sem(f"group1_stored{n}") for n in range(2)]
        early_stored = sem("early_stored")
        raw_loaded = [sem(f"raw_loaded_{name}") for name in ("ih", "hh")]
        w_hi_ready = sem("w_hi_ready")
        w_lo_ready = sem("w_lo_ready")
        w_lo_pool_ready = sem("w_lo_pool_ready")
        h0_loaded = sem("h0_loaded")
        x0_stored_loaded = sem("x0_stored_loaded")
        x0_kept_ready = sem("x0_kept_ready")
        bias_ih_loaded = sem("bias_ih_loaded")
        bias_hh_loaded = sem("bias_hh_loaded")
        bias_rz_ready = sem("bias_rz_ready")
        xT0_done = sem("xT0_done")
        xT0_hi_ready = sem("xT0_hi_ready")
        xT0_lo_ready = sem("xT0_lo_ready")
        xt_loaded = [sem(f"xt_loaded{n}") for n in range(RING)]
        x_quads_loaded = [sem(f"x_quads_loaded{n}") for n in range(RING)]
        xT_ready = sem("xT_ready")
        xT_hi_ready = sem("xT_hi_ready")
        xT_lo_ready = sem("xT_lo_ready")
        hT_done = sem("hT_done")
        hT_hi_ready = sem("hT_hi_ready")
        hT_lo_ready = sem("hT_lo_ready")
        gi_done = sem("gi_done")
        gh_r_done = sem("gh_r_done")
        gh_n_done = sem("gh_n_done")
        gh_z_done = sem("gh_z_done")
        new_x_ready = sem("new_x_ready")
        pre_r_ready = sem("pre_r_ready")
        r_ready = sem("r_ready")
        new_h_ready = sem("new_h_ready")
        reset_h_ready = sem("reset_h_ready")
        pre_n_ready = sem("pre_n_ready")
        n_ready = sem("n_ready")
        h_less_n_ready = sem("h_less_n_ready")
        pre_z_ready = sem("pre_z_ready")
        z_ready = sem("z_ready")
        z_part_ready = sem("z_part_ready")
        h_ready = sem("h_ready")
        out_ready = sem("out_ready")
        out_stored = [sem(f"out_stored{n}") for n in range(RING)]

        ROUNDS = T // RING
        assert T % RING == 0 and ROUNDS >= 3

        def rounds(eng, peel_first, body):
            if peel_first:
                for u in range(RING):
                    body(0, u)
            with eng.Fori(1 if peel_first else 0, ROUNDS - 1) as i:
                for u in range(RING):
                    body(i, u)
            for u in range(RING):
                body(ROUNDS - 1, u)

        def first(i, u):
            return not isinstance(i, bass.RuntimeValue) and i == 0 and u == 0

        def last(i, u):
            return not isinstance(i, bass.RuntimeValue) and i == ROUNDS - 1 and u == RING - 1

        def split_order(which):
            parts = [(k, g) for k in range(KB) for g in (R, Z, N)] if which == 0 else \
                    [(k, g) for g in (R, N, Z) for k in range(KB)]
            return [(k, g, slice(k * NG + g, k * NG + g + D)) for k, g in parts]

        def on_pool(which, k, g):
            return (k > 0 and g == N) if which == 0 else (k >= 2 and g == Z)

        def number(which, k, g):
            parts = [(w, kk, gg) for w in range(which + 1) for kk, gg, _ in split_order(w)]
            parts = parts[:parts.index((which, k, g)) + 1]
            return sum(on_pool(*part) == on_pool(which, k, g) for part in parts)

        LOW_DVE, LOW_POOL = number(1, 1, Z), number(1, KB - 1, Z)

        def low_weights(eng, which, cols):
            return eng.tensor_tensor(lo[which][:, cols], raw[which][:, cols],
                                     hi[which][:, cols].bitcast(F32), ALU.subtract)

        def to_toeplitz(copy, u):
            start = toep_span[:, u * PIECE:(u + 1) * PIECE]
            both = bass.AP(start.tensor, start.offset,
                           [start.ap[0], [to_toep0, CH], [T * PIECE, P // PIECE], [1, PIECE]])
            return copy(both, bank[u % 8][:, 0:CH * P].rearrange("p (c n i) -> p c n i", c=CH, i=PIECE),
                        in_matrix[:, u:u + 1])

        def load_taps(eng, half):
            of_both = taps[K - T:K, :].rearrange("s (c h i) -> s h c i", c=CH, h=2)[:, half]
            eng.dma_start(taps_sb[half * T:(half + 1) * T, :].rearrange("s (c i) -> s c i", c=CH),
                          of_both).then_inc(taps_loaded, 16)

        def store_times(eng, g, u0, u1, done):
            columns = slice(u0 * 2 * SLICE, u1 * 2 * SLICE)
            eng.dma_start(xres[g % 2, g // 2, :, u0:u1, :].rearrange("b u e -> b (u e)"),
                          stage(g)[:, columns]).then_inc(done, 16)

        late_groups = range(GROUPS, CH * GROUPS)

        block = ctx.enter_context(nc.Block())

        @block.sync
        def _(sp):
            def load_x(c, b0, b1):
                for half in range(2):
                    ch = (2 * c + half) * P
                    sp.dma_start(
                        x_sb[c][half * T:(half + 1) * T, b0 * P:b1 * P].rearrange("s (b i) -> s b i", i=P),
                        x[b0:b1, :, ch:ch + P].rearrange("b s i -> s b i"),
                    ).then_inc(x_loaded[c], 16)

            def load_weights(which, w):
                for k in range(KB):
                    for q in range(1 if which else QUADS):
                        row, rows = (k * P, P) if which else (first_channel(k, q), SLICE)
                        sp.dma_start(raw[which][q * rows:(q + 1) * rows, k * NG:(k + 1) * NG],
                                     w[row:row + rows, :]).then_inc(raw_loaded[which], 16)

            def load_xt(u, back):
                for g in range(2):
                    sp.dma_start(
                        xt[u][:, :].rearrange("b (k g e) -> b g k e", k=KB, g=2)[:, g],
                        xres[g, :, :, bass.ds(back, 1), :].rearrange("k b o e -> b k (o e)"),
                    ).then_inc(xt_loaded[u], 16)

            def load_x_quads(u, back):
                for q in range(QUADS):
                    g, e = q // 2, q % 2 * SLICE
                    sp.dma_start(
                        x_quads[u][q * SLICE:(q + 1) * SLICE, :].rearrange("p (w a) -> p w a", a=SLICE),
                        xres[g, :, :, bass.ds(back, 1), e:e + SLICE].rearrange(
                            "k (Q p) o a -> p (k Q) (o a)", Q=QUADS),
                    ).then_inc(x_quads_loaded[u], 16)

            load_taps(sp, 0)
            load_x(0, 0, B)
            load_x(1, 0, 3 * QUARTER)
            sp.wait_ge(stage_ready, GROUP_BANKS)
            store_times(sp, 0, 0, T // 2, group0_stored[0])
            sp.wait_ge(stage_ready, 2 * GROUP_BANKS)
            for n in range(2):
                store_times(sp, 1, n * T // 2, (n + 1) * T // 2, group1_stored[n])
            for n in range(2):
                sp.wait_ge(group1_stored[n], 16)
                load_x(1, 3 * QUARTER + n * QUARTER // 2, 3 * QUARTER + (n + 1) * QUARTER // 2)
            sp.wait_ge(stage_ready, 3 * GROUP_BANKS)
            store_times(sp, 2, 0, T, xres_stored[2])
            store_times(sp, 0, T // 2, T, group0_stored[1])
            sp.wait_ge(stage_ready, 4 * GROUP_BANKS)
            store_times(sp, 3, 0, T, xres_stored[3])

            sp.wait_ge(diag_ready, NPIECE // CH)
            sp.wait_ge(xres_stored[2], 16)
            load_weights(0, w_ih)
            sp.dma_start(h[:, :], taps).then_inc(h0_loaded, 16)
            sp.wait_ge(xres_stored[3], 16)
            for n in range(2):
                sp.wait_ge(group0_stored[n], 16)
            for g in range(2):
                sp.dma_start(x0_stored[:, :].rearrange("b (k g e) -> b g k e", g=2, e=2 * SLICE)[:, g],
                             xres[g, 0:KB // CH, :, T - 1, :].rearrange("k b e -> b k e"),
                             ).then_inc(x0_stored_loaded, 16)
            load_weights(1, w_hh)

            sp.wait_ge(w_lo_ready, number(0, KB - 1, Z))
            sp.wait_ge(w_lo_pool_ready, number(0, KB - 1, N))
            sp.dma_start(bias_ih[:, :], b_ih.partition_broadcast(P)).then_inc(bias_ih_loaded, 16)
            sp.wait_ge(early_stored, 16 * len(late_groups))
            load_x_quads(1, T - 2)
            sp.dma_start(bias_hh[:, :], b_hh.partition_broadcast(P)).then_inc(bias_hh_loaded, 16)
            load_xt(0, T - 1)
            load_x_quads(2, T - 3)
            for g in late_groups[:2]:
                store_times(sp, g, 0, T - RING, xres_stored[g])
            sp.wait_ge(xres_stored[GROUPS], 16)
            sp.wait_ge(x0_kept_ready, 1)
            load_x_quads(3, T - 4)
            for t in (1, 2, 3):
                load_xt(t, T - 1 - t)
            for g in late_groups[2:]:
                store_times(sp, g, 0, T - RING, xres_stored[g])
            for g in late_groups[1:]:
                sp.wait_ge(xres_stored[g], 16)

            def step(i, u):
                t = i * RING + u
                sp.wait_ge(out_ready, t + 1)
                sp.dma_start(out[:, bass.ds(t, 1), :].rearrange("b o d -> b (o d)"),
                             out_t[u][:, :]).then_inc(out_stored[u], 16)
                if isinstance(i, bass.RuntimeValue) or i < ROUNDS - 1:
                    load_xt(u, T - 1 - RING - u - i * RING)
                    load_x_quads(u, T - 1 - RING - u - i * RING)

            rounds(sp, False, step)
            for u in range(RING):
                sp.wait_ge(out_stored[u], 16 * ROUNDS)

        @block.gpsimd
        def _(pool):
            def ones_where(out, base, pattern):
                return nc.gpsimd.affine_select(out=out, in_=out, compare_op=ALU.not_equal, fill=1.0, base=base,
                                               pattern=pattern, channel_multiplier=1)

            nc.gpsimd.memset(lag0_row[:, :], 0.0).then_inc(lag0_row_set, 1)
            for n in range(2):
                pool.wait_ge(lag0_row_set, n + 1)
                ones_where(lag0_row[:, :], 1 - (n + 1) * T, [[0, 1]]).then_inc(lag0_row_set, 1)
            nc.gpsimd.memset(ident[:, :], 0.0).then_inc(ident_set, 1)
            pool.wait_ge(ident_set, 1)
            ones_where(ident[:, :], 0, [[-1, P + T]]).then_inc(ident_set, 1)
            nc.gpsimd.memset(in_matrix[:, :], 1.0).then_inc(in_matrix_set, 1)
            pool.wait_ge(in_matrix_set, 1)
            nc.gpsimd.affine_select(out=in_matrix[0:T, :], in_=in_matrix[0:T, :], compare_op=ALU.is_ge, fill=0.0,
                                    base=T - 1, pattern=[[-1, T]], channel_multiplier=-1).then_inc(in_matrix_set, 1)
            pool.wait_ge(in_matrix_set, 2)
            for n in range(2):
                nc.gpsimd.memset(diag[n][:, :], 0.0).then_inc(diag_zeroed, 1)

            for which in range(2):
                for n, (k, g, cols) in enumerate(split_order(which)):
                    if on_pool(which, k, g):
                        pool.wait_ge(w_hi_ready, which * KB * 3 + n + 1)
                        low_weights(nc.gpsimd, which, cols).then_inc(w_lo_pool_ready, 1)

            pool.wait_ge(bias_ih_loaded, 16)
            pool.wait_ge(bias_hh_loaded, 16)
            pool.wait_ge(w_lo_pool_ready, LOW_POOL)
            pool.wait_ge(w_lo_ready, number(0, KB - 1, Z))
            for g in (R, Z):
                nc.gpsimd.tensor_tensor(bias_rz[:, g:g + D], bias_ih[:, g:g + D], bias_hh[:, g:g + D],
                                        ALU.add).then_inc(bias_rz_ready, 1)

        @block.scalar
        def _(act):
            load_taps(act, 1)
            act.dma_start(conv_bias[:, :], conv_b.partition_broadcast(P)).then_inc(bias_loaded, 16)
            act.wait_ge(ident_set, 2)
            nc.scalar.activation(window[:, :], ident[:, :], ACT.Copy).then_inc(window_ready, 1)
            act.wait_ge(taps_plus_ready, CH)
            nc.scalar.activation(taps_hi[:, :], taps_plus[:, :], ACT.Copy).then_inc(taps_hi_ready, 1)
            act.wait_ge(in_matrix_set, 2)

            for u in range(0, T, 2):
                act.wait_ge(shift_done, u + 1)
                to_toeplitz(lambda o, i, m: nc.scalar.activation(o, i, ACT.Identity, scale=m),
                            u).then_inc(toep_even_ready, 1)

            act.wait_ge(diag_zeroed, 2)
            for p in range(NPIECE):
                c, i0 = p // (NPIECE // CH), p % (NPIECE // CH) * PIECE
                if p == 0:
                    act.wait_ge(toep_even_ready, T // 2)
                    act.wait_ge(toep_odd_ready, T // 2)
                if p >= 2:
                    act.wait_ge(conv_done, (p - 1) * PBANKS)
                for half in range(2):
                    rows = slice(half * T, (half + 1) * T)
                    m = nc.scalar.activation(
                        diag[p % 2][rows, :].rearrange("s (i h u) -> s i h u", i=PIECE, h=2)[:, :, half, :],
                        toep[c][rows, i0 * T:(i0 + PIECE) * T].rearrange("s (u i) -> s i u", u=T), ACT.Copy)
                m.then_inc(diag_ready, 1)

            def x0_hi(half):
                cols = slice(half * D // 2, (half + 1) * D // 2)
                act.wait_ge(xT0_done, half + 1)
                nc.scalar.activation(xT_hi[:, cols], ps_x0[half][:, 0:D // 2], ACT.Copy).then_inc(xT0_hi_ready, 1)

            act.wait_ge(conv_done, NBANK)
            x0_hi(0)
            for which in range(2):
                act.wait_ge(raw_loaded[which], 16 * KB * (1 if which else QUADS))
                for n, (k, g, cols) in enumerate(split_order(which)):
                    nc.scalar.activation(hi[which][:, cols], raw[which][:, cols], ACT.Copy).then_inc(w_hi_ready, 1)
                    if which == 0 and n == 2:
                        act.wait_ge(stage_ready, NBANK)
                        for late in late_groups:
                            store_times(act, late, T - RING, T, early_stored)
                    if which == 0 and n == 4:
                        x0_hi(1)
                    if which == 0 and n == 6:
                        act.wait_ge(hT_done, 1)
                        nc.scalar.activation(hT_hi[:, :], ps_hT[:, :], ACT.Copy).then_inc(hT_hi_ready, 1)

            def step(i, u):
                t = i * RING + u
                if not last(i, u):
                    act.wait_ge(gi_done, t + 1)
                    act.wait_ge(xT_ready, t + 1)
                    nc.scalar.activation(xT_hi[:, :], xT[:, :], ACT.Copy).then_inc(xT_hi_ready, 1)
                act.wait_ge(pre_r_ready, t + 1)
                nc.scalar.activation(r[:, :], pre_r[:, :], ACT.Sigmoid).then_inc(r_ready, 1)
                act.wait_ge(pre_n_ready, t + 1)
                nc.scalar.activation(n_gate[:, :], pre_n[:, :], ACT.Tanh).then_inc(n_ready, 1)
                act.wait_ge(pre_z_ready, t + 1)
                nc.scalar.activation(z[:, :], pre_z[:, :], ACT.Sigmoid).then_inc(z_ready, 1)
                if not last(i, u):
                    act.wait_ge(hT_done, t + 2)
                    nc.scalar.activation(hT_hi[:, :], ps_hT[:, :], ACT.Copy).then_inc(hT_hi_ready, 1)

            rounds(act, False, step)

        @block.vector
        def _(dve):
            dve.wait_ge(taps_loaded, 16 * 2)
            dve.wait_ge(lag0_row_set, 3)
            for c in range(CH):
                nc.vector.tensor_scalar(taps_plus[:, (1 - c) * P:(2 - c) * P], taps_sb[:, c * P:(c + 1) * P],
                                        lag0_row[:, 0:1], None, ALU.add).then_inc(taps_plus_ready, 1)
            dve.wait_ge(taps_hi_ready, 1)
            nc.vector.tensor_tensor(taps_lo[:, :], taps_plus[:, :], taps_hi[:, :].bitcast(F32),
                                    ALU.subtract).then_inc(taps_lo_ready, 1)
            dve.wait_ge(in_matrix_set, 2)

            for u in range(1, T, 2):
                dve.wait_ge(shift_done, u + 1)
                to_toeplitz(lambda o, i, m: nc.vector.tensor_scalar(o, i, m, None, ALU.mult),
                            u).then_inc(toep_odd_ready, 1)
            dve.wait_ge(bias_loaded, 16)

            def low_part(lo_out, full, hi_in, hi_ready, lo_ready, count):
                dve.wait_ge(hi_ready, count)
                nc.vector.tensor_tensor(lo_out[:, :], full[:, :], hi_in[:, :].bitcast(F32),
                                        ALU.subtract).then_inc(lo_ready, 1)

            for m in range(NBANK):
                g, i0 = m // GROUP_BANKS, m % GROUP_BANKS * BPAIRS
                c = g // GROUPS
                dve.wait_ge(conv_done, m + 1)
                if i0 == 0 and g == GROUPS - 1:
                    dve.wait_ge(conv_done, (g + 1) * GROUP_BANKS)
                if i0 == 0 and g == CH * GROUPS - 1:
                    dve.wait_ge(xres_stored[GROUPS - 1], 16)
                i1 = (g % GROUPS) * SLICE + i0
                bias = conv_bias[:, c * 2 * P:(c + 1) * 2 * P].rearrange("b (h i) -> b i h", h=2)
                nc.vector.tensor_tensor(
                    stage(g).rearrange("b (u h i) -> b i h u", h=2, i=SLICE)[:, i0:i0 + BPAIRS],
                    bank[m % 8][:, :].rearrange("b (i h u) -> b i h u", i=BPAIRS, h=2),
                    bias[:, i1:i1 + BPAIRS, :].unsqueeze(3).to_broadcast([P, BPAIRS, 2, T]),
                    ALU.add,
                ).then_inc(stage_ready, 1)

            dve.wait_ge(stage_ready, NBANK)
            nc.vector.tensor_copy(
                x0_kept[:, :].rearrange("b (g e) -> b g e", g=GROUPS),
                kept[:, :].rearrange("b (g u e) -> b g u e", g=GROUPS, u=T)[:, :, T - 1, :],
            ).then_inc(x0_kept_ready, 1)

            def x0_lo(half):
                cols = slice(half * D // 2, (half + 1) * D // 2)
                dve.wait_ge(xT0_hi_ready, half + 1)
                nc.vector.tensor_tensor(xT_lo[:, cols], ps_x0[half][:, 0:D // 2], xT_hi[:, cols].bitcast(F32),
                                        ALU.subtract).then_inc(xT0_lo_ready, 1)

            x0_lo(0)
            for which in range(2):
                for n, (k, g, cols) in enumerate(split_order(which)):
                    if not on_pool(which, k, g):
                        dve.wait_ge(w_hi_ready, which * KB * 3 + n + 1)
                        low_weights(nc.vector, which, cols).then_inc(w_lo_ready, 1)
                    if which == 0 and n == 4:
                        x0_lo(1)
                    if which == 0 and n == 8:
                        low_part(hT_lo, ps_hT, hT_hi, hT_hi_ready, hT_lo_ready, 1)

            def step(i, u):
                t = i * RING + u
                if not last(i, u):
                    nxt = (u + 1) % RING
                    dve.wait_ge(x_quads_loaded[nxt], 16 * QUADS * (i + 1))
                    if not first(i, u):
                        dve.wait_ge(xT_lo_ready, t)
                    nc.vector.transpose(xT[:, :], x_quads[nxt][:, :]).then_inc(xT_ready, 1)
                if first(i, u):
                    dve.wait_ge(bias_ih_loaded, 16)
                    dve.wait_ge(w_lo_pool_ready, LOW_POOL)
                dve.wait_ge(gi_done, t + 1)
                nc.vector.tensor_tensor(new_x[:, :], ps_in[:, :], bias_ih[:, N:NG], ALU.add).then_inc(new_x_ready, 1)
                if not last(i, u):
                    low_part(xT_lo, xT, xT_hi, xT_hi_ready, xT_lo_ready, t + 1)
                if first(i, u):
                    dve.wait_ge(bias_rz_ready, 1)
                dve.wait_ge(gh_r_done, t + 1)
                nc.vector.tensor_tensor(pre_r[:, :], ps_r[:, :], bias_rz[:, R:R + D], ALU.add).then_inc(pre_r_ready, 1)
                dve.wait_ge(gh_n_done, t + 1)
                nc.vector.tensor_tensor(new_h[:, :], ps_hn[:, :], bias_hh[:, N:NG], ALU.add).then_inc(new_h_ready, 1)
                dve.wait_ge(new_h_ready, t + 1)
                dve.wait_ge(r_ready, t + 1)
                nc.vector.tensor_tensor(reset_h[:, :], new_h[:, :], r[:, :], ALU.mult).then_inc(reset_h_ready, 1)
                dve.wait_ge(reset_h_ready, t + 1)
                nc.vector.tensor_tensor(pre_n[:, :], reset_h[:, :], new_x[:, :], ALU.add).then_inc(pre_n_ready, 1)
                if first(i, u):
                    dve.wait_ge(bias_rz_ready, 2)
                dve.wait_ge(gh_z_done, t + 1)
                nc.vector.tensor_tensor(pre_z[:, :], ps_z[:, :], bias_rz[:, Z:Z + D], ALU.add).then_inc(pre_z_ready, 1)
                dve.wait_ge(n_ready, t + 1)
                nc.vector.tensor_tensor(h_less_n[:, :], h[:, :], n_gate[:, :],
                                        ALU.subtract).then_inc(h_less_n_ready, 1)
                dve.wait_ge(h_less_n_ready, t + 1)
                dve.wait_ge(z_ready, t + 1)
                nc.vector.tensor_tensor(h_less_n[:, :], z[:, :], h_less_n[:, :], ALU.mult).then_inc(z_part_ready, 1)
                dve.wait_ge(z_part_ready, t + 1)
                nc.vector.tensor_tensor(h[:, :], n_gate[:, :], h_less_n[:, :], ALU.add).then_inc(h_ready, 1)
                dve.wait_ge(h_ready, t + 1)
                dve.wait_ge(xt_loaded[u], 32 * (i + 1))
                if isinstance(i, bass.RuntimeValue) or i > 0:
                    dve.wait_ge(out_stored[u], 16 * i)
                for c in range(CH):
                    m = nc.vector.tensor_tensor(
                        out_t[u][:, c * 2 * P:(c + 1) * 2 * P].rearrange("b (h g i) -> b h g i", h=2, g=GROUPS),
                        xt[u][:, c * 2 * P:(c + 1) * 2 * P].rearrange("b (g h i) -> b h g i", h=2, g=GROUPS),
                        h[:, c * 2 * P:(c + 1) * 2 * P].rearrange("b (h g i) -> b h g i", h=2, g=GROUPS),
                        ALU.add)
                m.then_inc(out_ready, 1)
                if not last(i, u):
                    low_part(hT_lo, ps_hT, hT_hi, hT_hi_ready, hT_lo_ready, t + 2)

            dve.wait_ge(h0_loaded, 16)
            dve.wait_ge(w_lo_ready, LOW_DVE)
            rounds(dve, True, step)

        @block.tensor
        def _(pe):
            pe.wait_ge(window_ready, 1)
            pe.wait_ge(taps_lo_ready, 1)

            for u in range(T):
                if u >= 8:
                    pe.wait_ge(toep_odd_ready if u % 2 else toep_even_ready, (u - 8) // 2 + 1)
                for part in (taps_hi, taps_lo):
                    mm = nc.tensor.matmul(bank[u % 8][:, 0:CH * P], window[:, u:u + P], part[:, :],
                                          start=part is taps_hi, stop=part is taps_lo)
                mm.then_inc(shift_done, 1)
            pe.wait_ge(toep_even_ready, T // 2)
            pe.wait_ge(toep_odd_ready, T // 2)

            for p in range(NPIECE):
                c, i0 = p // (NPIECE // CH), p % (NPIECE // CH) * PIECE
                if i0 == 0:
                    pe.wait_ge(x_loaded[c], 16 * 2 * (3 if c else 1))
                pe.wait_ge(diag_ready, p + 1)
                for j in range(PIECE):
                    m = (p * PIECE + j) // BPAIRS
                    if j % BPAIRS == 0 and m >= 8:
                        pe.wait_ge(stage_ready, m - 7)
                    mm = nc.tensor.matmul(
                        bank[m % 8][:, j % BPAIRS * P:(j % BPAIRS + 1) * P],
                        x_sb[c][:, :].rearrange("s (b i) -> s i b", b=B)[:, i0 + j, :],
                        diag[p % 2][:, j * P:(j + 1) * P], start=True, stop=True)
                    if j % BPAIRS == BPAIRS - 1:
                        mm.then_inc(conv_done, 1)

            def transpose(psum, done, block_of):
                for k in range(KB):
                    mm = nc.tensor.transpose(psum[:, k * P:(k + 1) * P], block_of(k), ident[:, 0:P])
                mm.then_inc(done, 1)

            def h_block(k):
                return h[:, k * P:(k + 1) * P]

            def block_product(psum, part_hi, part_lo, which, gate, k, start, stop):
                rows = slice(k * P, (k + 1) * P)
                cols = slice(k * NG + gate, k * NG + gate + D)
                for n, (a, w) in enumerate(((part_hi, hi), (part_hi, lo), (part_lo, hi))):
                    mm = nc.tensor.matmul(psum[:, :], a[:, rows], w[which][:, cols],
                                          start=start and n == 0, stop=stop and n == 2)
                return mm

            def product(psum, part_hi, part_lo, which, gate, start, stop):
                for k in range(KB):
                    mm = block_product(psum, part_hi, part_lo, which, gate, k,
                                       start and k == 0, stop and k == KB - 1)
                return mm

            def x_product(psum, gate, stop):
                return product(psum, xT_hi, xT_lo, 0, gate, True, stop)

            def h_product(psum, gate, start):
                return product(psum, hT_hi, hT_lo, 1, gate, start, True)

            def low_weights_ready(which, k, gate):
                pe.wait_ge(w_lo_pool_ready if on_pool(which, k, gate) else w_lo_ready, number(which, k, gate))

            def transpose_x0(half, x0):
                for k in range(KB // 2):
                    mm = nc.tensor.transpose(ps_x0[half][:, k * P:(k + 1) * P], x0[:, k * P:(k + 1) * P],
                                             ident[:, 0:P])
                mm.then_inc(xT0_done, 1)

            pe.wait_ge(ident_set, 2)
            pe.wait_ge(x0_stored_loaded, 32)
            pe.wait_ge(stage_ready, NBANK - 3)
            transpose_x0(0, x0_stored)
            pe.wait_ge(h0_loaded, 16)
            pe.wait_ge(stage_ready, NBANK - 2)
            transpose(ps_hT, hT_done, h_block)
            pe.wait_ge(stage_ready, NBANK)
            pe.wait_ge(x0_kept_ready, 1)
            transpose_x0(1, x0_kept)
            for k in range(KB):
                pe.wait_ge(xT0_lo_ready, k // 2 + 1)
                for psum, gate, stop in ((ps_r, R, False), (ps_z, Z, False), (ps_in, N, True)):
                    low_weights_ready(0, k, gate)
                    mm = block_product(psum, xT_hi, xT_lo, 0, gate, k, k == 0, stop and k == KB - 1)
            mm.then_inc(gi_done, 1)

            def weights_ready(i, u, gate):
                if first(i, u):
                    for k in range(KB):
                        low_weights_ready(1, k, gate)

            def step(i, u):
                t = i * RING + u
                pe.wait_ge(hT_lo_ready, t + 1)
                weights_ready(i, u, R)
                h_product(ps_r, R, False).then_inc(gh_r_done, 1)
                weights_ready(i, u, N)
                h_product(ps_hn, N, True).then_inc(gh_n_done, 1)
                weights_ready(i, u, Z)
                h_product(ps_z, Z, False).then_inc(gh_z_done, 1)
                if not last(i, u):
                    pe.wait_ge(xT_lo_ready, t + 1)
                    pe.wait_ge(pre_r_ready, t + 1)
                    x_product(ps_r, R, False)
                    pe.wait_ge(new_x_ready, t + 1)
                    x_product(ps_in, N, True)
                    pe.wait_ge(h_ready, t + 1)
                    transpose(ps_hT, hT_done, h_block)
                    pe.wait_ge(pre_z_ready, t + 1)
                    x_product(ps_z, Z, False).then_inc(gi_done, 1)

            rounds(pe, True, step)


_INS = ["x", "cond_2048", "L0_cond_b", "L1_cond_W_ih", "L1_cond_W_hh", "L1_cond_b_ih", "L1_cond_b_hh"]
_OUTS = [((128, 64, 512), "float32")]


def kernel(**inputs):
    import numpy as _np
    import concourse.bacc as _bacc
    from concourse import mybir as _mybir
    from concourse.bass_utils import run_bass_kernel_spmd as _run

    nc = _bacc.Bacc("TRN2", target_bir_lowering=False, num_devices=1, dynamic_dma_scratch_size=1024)
    arrays, args = {}, []
    for name in _INS:
        a = _np.ascontiguousarray(inputs[name])
        arrays[f"in_{name}_dram"] = a
        args.append(nc.dram_tensor(f"in_{name}_dram", a.shape, _mybir.dt.from_np(a.dtype), kind="ExternalInput").ap())
    for i, (shape, dtype) in enumerate(_OUTS):
        dt = _mybir.dt.from_np(_np.dtype(dtype))
        args.append(nc.dram_tensor(f"out_{i}_dram", shape, dt, kind="ExternalOutput").ap())
    conv_residual_gru(nc, *args)
    r = _run(nc, [arrays], core_ids=[0])
    return r.results[0]["out_0_dram"]
```
